# Optimizing a Trainium2 kernel written in Bass

```python
import numpy as np
import jax
import jax.numpy as jnp

def _softmax(x, axis=-1):
    return jax.nn.softmax(x, axis=axis)

def _gelu(x):
    return jax.nn.gelu(x, approximate=True)

def _silu(x):
    return jax.nn.silu(x)

def _sigmoid(x):
    return jax.nn.sigmoid(x)

def _layernorm(x, axis=-1, eps=1e-05):
    m = jnp.mean(x, axis=axis, keepdims=True)
    v = jnp.var(x, axis=axis, keepdims=True)
    return (x - m) / jnp.sqrt(v + eps)

def _scatter_add(tgt, idx, src, axis=0):
    return tgt.at[idx].add(src)

def _segment_sum(src, seg, n):
    return jax.ops.segment_sum(src, seg, n)
kernel_name = 'mk_flamingo_gated_d1_seqx_r4_84fd6c'

def setup_inputs(seed: int=0):
    np.random.seed(seed)
    _w = jnp.asarray

    def _rec_inputs():
        import jax
        import jax.numpy as jnp
        _rk = jax.random.key(seed)
        x = -0.0003929 + 0.9999 * jax.random.normal(jax.random.fold_in(_rk, 1), (4, 1024, 256), jnp.float32)
        _lenS = 1024 - jax.random.randint(jax.random.fold_in(_rk, 7), (4,), 0, max(1, 1024 // 4) + 1, jnp.int32)
        _lenS2 = 77 - jax.random.randint(jax.random.fold_in(_rk, 8), (4,), 0, max(1, 77 // 4) + 1, jnp.int32)
        _ctx_768P = jax.random.normal(jax.random.fold_in(_rk, 11), (4, 16, 192), jnp.float32)
        _ctx_768c = jax.random.dirichlet(jax.random.fold_in(_rk, 511), 0.3 * jnp.ones((16,), jnp.float32), (4, 77))
        _ctx_768t = jnp.einsum('bsk,bkd->bsd', _ctx_768c, _ctx_768P)
        _ctx_768t = _ctx_768t * jax.lax.rsqrt(jnp.mean(jnp.square(_ctx_768t)) + 1e-12) * 0.953939
        ctx_768 = -7.36909e-05 + 0.999899 * (_ctx_768t + 0.3 * jax.random.normal(jax.random.fold_in(_rk, 611), (4, 77, 192), jnp.float32))
        _g = jax.random.normal(jax.random.fold_in(_rk, 9001), (2, 1), jnp.float32)
        _g = jnp.sign(_g) * jnp.maximum(jnp.abs(_g), 1.0) + (_g == 0) * 1.0
        g_xattn = _g[0]
        g_ffn = _g[1]
        return (x, ctx_768, g_xattn, g_ffn)
    x, ctx_768, g_xattn, g_ffn = _rec_inputs()

    def _L0_xattn_setup():
        import jax, jax.numpy as jnp
        import numpy as np
        EPS = 1e-05

        def layernorm(x, g, b):
            mu = jnp.mean(x, axis=-1, keepdims=True)
            var = jnp.mean(jnp.square(x - mu), axis=-1, keepdims=True)
            return (x - mu) * jax.lax.rsqrt(var + EPS) * g + b
        key = jax.random.key(seed)
        ks = jax.random.split(key, 12)
        B, L1, L2 = (8, 512, 512)
        D1, D2, E = (256, 192, 256)
        s1, s2, se = (D1 ** (-0.5), D2 ** (-0.5), E ** (-0.5))
        return {'modality1': jax.random.normal(ks[0], (B, L1, D1), jnp.float32), 'modality2': jax.random.normal(ks[1], (B, L2, D2), jnp.float32), 'ln1_g': jnp.ones((D1,), jnp.float32), 'ln1_b': jnp.zeros((D1,), jnp.float32), 'ln2_g': jnp.ones((D2,), jnp.float32), 'ln2_b': jnp.zeros((D2,), jnp.float32), 'Wq': jax.random.normal(ks[2], (D1, E), jnp.float32) * s1, 'bq': jax.random.normal(ks[3], (E,), jnp.float32) * 0.01, 'Wk': jax.random.normal(ks[4], (D2, E), jnp.float32) * s2, 'bk': jax.random.normal(ks[5], (E,), jnp.float32) * 0.01, 'Wv': jax.random.normal(ks[6], (D2, E), jnp.float32) * s2, 'bv': jax.random.normal(ks[7], (E,), jnp.float32) * 0.01, 'Wo': jax.random.normal(ks[8], (E, D1), jnp.float32) * se, 'bo': jax.random.normal(ks[9], (D1,), jnp.float32) * 0.01}
    _L0_xattn_all = _L0_xattn_setup()
    _L0_xattn_in = {k: v for k, v in _L0_xattn_all.items() if k in ('ln1_g', 'ln1_b', 'ln2_g', 'ln2_b', 'Wq', 'bq', 'Wk', 'bk', 'Wv', 'bv', 'Wo', 'bo')}
    del _L0_xattn_all

    def _L0_ffn_setup():
        import jax, jax.numpy as jnp
        import numpy as np
        B, S, D, H, E = (2, 512, 256, 1024, 8)
        TOP_K = 2
        key = jax.random.key(seed)
        ks = jax.random.split(key, 5)
        scale = 0.02
        return {'x': jax.random.normal(ks[0], (B, S, D), dtype=jnp.float32), 'gate_w': jax.random.normal(ks[1], (D, E), dtype=jnp.float32) * scale, 'gate_b': jnp.zeros((E,), dtype=jnp.float32), 'w1': jax.random.normal(ks[2], (E, D, H), dtype=jnp.float32) * scale, 'b1': jnp.zeros((E, H), dtype=jnp.float32), 'w2': jax.random.normal(ks[3], (E, H, D), dtype=jnp.float32) * scale, 'b2': jnp.zeros((E, D), dtype=jnp.float32)}
    _L0_ffn_all = _L0_ffn_setup()
    _L0_ffn_in = {k: v for k, v in _L0_ffn_all.items() if k in ('gate_w', 'gate_b', 'w1', 'b1', 'w2', 'b2')}
    del _L0_ffn_all
    return {'x': x, 'ctx_768': ctx_768, 'g_xattn': g_xattn, 'g_ffn': g_ffn, 'L0_xattn_ln1_g': _L0_xattn_in['ln1_g'], 'L0_xattn_ln1_b': _L0_xattn_in['ln1_b'], 'L0_xattn_ln2_g': _L0_xattn_in['ln2_g'], 'L0_xattn_ln2_b': _L0_xattn_in['ln2_b'], 'L0_xattn_Wq': _L0_xattn_in['Wq'], 'L0_xattn_bq': _L0_xattn_in['bq'], 'L0_xattn_Wk': _L0_xattn_in['Wk'], 'L0_xattn_bk': _L0_xattn_in['bk'], 'L0_xattn_Wv': _L0_xattn_in['Wv'], 'L0_xattn_bv': _L0_xattn_in['bv'], 'L0_xattn_Wo': _L0_xattn_in['Wo'], 'L0_xattn_bo': _L0_xattn_in['bo'], 'L0_ffn_gate_w': _L0_ffn_in['gate_w'], 'L0_ffn_gate_b': _L0_ffn_in['gate_b'], 'L0_ffn_w1': _L0_ffn_in['w1'], 'L0_ffn_b1': _L0_ffn_in['b1'], 'L0_ffn_w2': _L0_ffn_in['w2'], 'L0_ffn_b2': _L0_ffn_in['b2']}

def reference(x, ctx_768, g_xattn, g_ffn, L0_xattn_ln1_g, L0_xattn_ln1_b, L0_xattn_ln2_g, L0_xattn_ln2_b, L0_xattn_Wq, L0_xattn_bq, L0_xattn_Wk, L0_xattn_bk, L0_xattn_Wv, L0_xattn_bv, L0_xattn_Wo, L0_xattn_bo, L0_ffn_gate_w, L0_ffn_gate_b, L0_ffn_w1, L0_ffn_b1, L0_ffn_w2, L0_ffn_b2):
    import jax
    import jax.numpy as jnp

    def _L0_xattn_ref(modality1, modality2, ln1_g, ln1_b, ln2_g, ln2_b, Wq, bq, Wk, bk, Wv, bv, Wo, bo):
        import jax, jax.numpy as jnp
        import numpy as np
        EPS = 1e-05

        def layernorm(x, g, b):
            mu = jnp.mean(x, axis=-1, keepdims=True)
            var = jnp.mean(jnp.square(x - mu), axis=-1, keepdims=True)
            return (x - mu) * jax.lax.rsqrt(var + EPS) * g + b
        E = Wq.shape[1]
        scaling = E ** (-0.5)
        x1 = layernorm(modality1, ln1_g, ln1_b)
        x2 = layernorm(modality2, ln2_g, ln2_b)
        q = x1 @ Wq + bq
        k = x2 @ Wk + bk
        v = x2 @ Wv + bv
        scores = jnp.einsum('bqe,bke->bqk', q, k) * scaling
        attn = jax.nn.softmax(scores, axis=-1)
        ctx = jnp.einsum('bqk,bke->bqe', attn, v)
        return ctx @ Wo + bo

    def _L0_ffn_ref(x, gate_w, gate_b, w1, b1, w2, b2):
        import jax, jax.numpy as jnp
        import numpy as np
        B, S, D, H, E = (2, 512, 256, 1024, 8)
        TOP_K = 2
        gate_logits = jnp.einsum('bsd,de->bse', x, gate_w) + gate_b
        gate_weights = jax.nn.softmax(gate_logits, axis=-1)
        topk_values, topk_indices = jax.lax.top_k(gate_weights, TOP_K)
        hidden = jax.nn.relu(jnp.einsum('bsd,edh->bseh', x, w1) + b1)
        expert_out = jnp.einsum('bseh,ehd->bsed', hidden, w2) + b2
        sel = jnp.take_along_axis(expert_out, topk_indices[..., None], axis=2)
        return jnp.sum(topk_values[..., None] * sel, axis=2)
    x = x + jnp.tanh(g_xattn[0]) * _L0_xattn_ref(_layernorm(x, axis=-1), ctx_768, L0_xattn_ln1_g, L0_xattn_ln1_b, L0_xattn_ln2_g, L0_xattn_ln2_b, L0_xattn_Wq, L0_xattn_bq, L0_xattn_Wk, L0_xattn_bk, L0_xattn_Wv, L0_xattn_bv, L0_xattn_Wo, L0_xattn_bo)
    x = x + jnp.tanh(g_ffn[0]) * _L0_ffn_ref(_layernorm(x, axis=-1), L0_ffn_gate_w, L0_ffn_gate_b, L0_ffn_w1, L0_ffn_b1, L0_ffn_w2, L0_ffn_b2)
    return x

_drawn_inputs = setup_inputs


def setup_inputs(seed=0):
    import zlib

    import numpy as np

    out = dict(_drawn_inputs(seed))
    spreads = {'L0_xattn_ln1_g': (1.0, 0.2),
     'L0_xattn_ln1_b': (0.0, 0.489),
     'L0_xattn_ln2_g': (1.0, 0.2),
     'L0_xattn_ln2_b': (0.0, 0.1),
     'L0_ffn_gate_b': (0.0, 0.361),
     'L0_ffn_b1': (0.0, 0.789),
     'L0_ffn_b2': (0.0, 0.358)}
    factors = {'L0_xattn_bq': 34.138, 'L0_xattn_bk': 64.0, 'L0_xattn_bv': 8.0, 'L0_xattn_bo': 7.398}
    for name, (base, spread) in spreads.items():
        noise = np.random.default_rng([zlib.crc32(name.encode()), seed]).standard_normal(out[name].shape)
        drawn = base * np.exp(spread * noise) if base else spread * noise
        out[name] = jnp.asarray(drawn.astype(out[name].dtype))
    for name, factor in factors.items():
        out[name] = (out[name] * factor).astype(out[name].dtype)
    return out
```

```python
import concourse.bass as bass
from concourse import mybir
from contextlib import ExitStack


def gated_attention_and_routed_experts(
    nc, x, ctx_768, g_xattn, g_ffn, ln1_g, ln1_b, ln2_g, ln2_b, Wq, bq, Wk, bk, Wv, bv, Wo, bo,
    gate_w, gate_b, w1, b1, w2, b2, out,
):
    F32, F16, I32, U32 = mybir.dt.float32, mybir.dt.float16, mybir.dt.int32, mybir.dt.uint32
    ALU = mybir.AluOpType
    ACT = mybir.ActivationFunctionType
    AX = mybir.AxisListType
    ds = bass.ds

    P = 128
    B, L, D = x.shape
    _, LC, DC = ctx_768.shape
    E, _, H = w1.shape
    KO = 2
    T = L // P
    NT = B * T
    ND = D // P
    NH = H // P
    NC = B * LC
    DC2 = DC - P
    JE = B * L // P
    NBLK = E * JE // P
    HT = 2
    PS = HT * P
    S = (KO * B * L + E * (PS - 1)) // PS
    SP = HT * S + 2
    XW = D + E
    EPS = 1e-5
    SCALE = float(Wq.shape[1]) ** -0.5
    EB = E // B
    U = 4
    LOOPS = (S - 3) // U
    HC = 512 // PS
    NHB = NH // HC
    assert ND == 2 and NBLK == 2 and B * L == 4096 and LC <= P and NC <= 512

    xrows = nc.dram_tensor("xrows", (B * L + P, XW), F32, kind="Internal").ap()
    sums = nc.dram_tensor("sums", (B * L + P, D), F32, kind="Internal").ap()

    with ExitStack() as ctx:
        def sb(name, shape, dt=F32):
            return ctx.enter_context(nc.sbuf_tensor(name, shape, dt))

        def sem(name):
            return ctx.enter_context(nc.semaphore(name))

        bank = [ctx.enter_context(nc.psum_tensor(f"bank{i}", [P, 512], F32)) for i in range(8)]

        w1h = sb("w1h", [P, E * ND * H], F16)
        w1l = sb("w1l", [P, E * ND * H], F16)
        w2h = sb("w2h", [P, E * NH * D], F16)
        w2l = sb("w2l", [P, E * NH * D], F16)
        RAW = ND * H + NH * D
        pool0 = sb("pool0", [P, 2 * RAW])
        raw = [pool0[:, i * RAW:(i + 1) * RAW] for i in range(2)]
        off = [0]

        def carve(n, dt=F32):
            words = n if dt == F32 else n // 2
            a = pool0[:, off[0]:off[0] + words]
            off[0] += words
            return a if dt == F32 else a.bitcast(dt)

        xh = [carve(ND * PS, F16) for _ in range(2)]
        xl = [carve(ND * PS, F16) for _ in range(2)]
        hh = [carve(NH * PS, F16) for _ in range(2)]
        hl = [carve(NH * PS, F16) for _ in range(2)]
        list_off = off[0]
        hb = [carve(512) for _ in range(NHB)]
        b1s = sb("b1s", [P, E * NH])
        b2s = sb("b2s", [P, E * D])
        inv = sb("inv", [P, E])
        idx_tab = sb("idx_tab", [P, SP], I32)
        idx_out = [sb(f"idx_out{i}", [P, 1], I32) for i in range(2 * HT)]
        idx = [sb(f"idx{i}", [P, 1], I32) for i in range(U * HT)]
        eid = sb("eid", [1, SP], I32)
        q = [sb(f"q{i}", [P, HT]) for i in range(U)]

        ident = sb("ident", [P, P])
        ones = sb("ones", [P, P])
        ones16 = sb("ones16", [P, P], F16)
        zero16 = sb("zero16", [P, P], F16)
        before16 = sb("before16", [P, P], F16)
        iotaR = sb("iotaR", [P, P], F16)
        iotaJ = sb("iotaJ", [P, E * JE], F16)
        iota_e = sb("iota_e", [P, E])
        iota_s = sb("iota_s", [P, SP])
        tokv = sb("tokv", [P, NT])
        incl = sb("incl", [P, E, E])
        own_e = sb("own_e", [P, NBLK, E])
        empty = sb("empty", [P, 1])
        pnum = sb("pnum", [P, 1])
        jpos = sb("jpos", [P, 1])
        jpos_i = sb("jpos_i", [P, 1], I32)
        neghalf = sb("neghalf", [P, T])
        half = sb("half", [P, 1])

        gates_in = sb("gates_in", [P, 2])
        tg = sb("tg", [P, 2])
        ln1c = sb("ln1c", [P, 2 * ND])
        ln1s = sb("ln1s", [P, ND])
        bqc = sb("bqc", [P, ND])
        bkc = sb("bkc", [P, ND])
        bvc = sb("bvc", [P, ND])
        gbr = sb("gbr", [P, E])
        gw_s = sb("gw_s", [P, ND, E])

        sc = w2l[:, (E - EB) * NH * D:E * NH * D].bitcast(F32)
        soff = [0]

        def scr(n):
            a = sc[:, soff[0]:soff[0] + n]
            soff[0] += n
            return a

        ctx_s = scr(B * DC).rearrange("p (b d) -> p b d", b=B)
        x2T = [scr(NC), scr(NC)]
        KT = [scr(NC), scr(NC)]
        WqT = w2h[:, (E - EB) * NH * D:E * NH * D].bitcast(F32)[:, 0:ND * D].rearrange("p (c d) -> p c d", c=ND)
        assert soff[0] <= EB * NH * D // 2
        sc2 = w1l[:, (E - EB) * ND * H:E * ND * H].bitcast(F32)
        Wk_s = sc2[:, 0:2 * D].rearrange("p (c d) -> p c d", c=2)
        Wv_s = sc2[:, 2 * D:4 * D].rearrange("p (c d) -> p c d", c=2)
        VT = [sc2[:, 4 * D:4 * D + NC], sc2[:, 4 * D + NC:4 * D + 2 * NC]]
        sc3 = w1h[:, (E - EB) * ND * H:E * ND * H].bitcast(F32)
        Wq_s = sc3[:, 0:ND * D].rearrange("p (c d) -> p c d", c=ND)
        Wo_s = sc3[:, ND * D:2 * ND * D].rearrange("p (c d) -> p c d", c=ND)
        ln2r = sc3[:, 2 * ND * D:2 * ND * D + 2 * DC].rearrange("p (c d) -> p c d", c=2)
        b1row = sc3[0:E * NH, 1536 + D:1536 + D + P]
        bor = sc3[:, 1536:1536 + D]
        uq = sb("uq", [P, ND])
        st2 = sb("st2", [P, B, 6])
        mv2 = sb("mv2", [P, B, 2])
        rs2 = sb("rs2", [P, B])

        KQ = [sb(f"KQ{c}", [P, NC]) for c in range(ND)]
        cst = sb("cst", [1, NC])
        VO = sb("VO", [P, B * D])

        xb = [sb(f"xb{i}", [P, T, D]) for i in range(1)]
        xext = sb("xext", [P, T, XW])
        xhat = [xext[:, i, 0:D] for i in range(T)]
        pr = [xext[:, i, 0:LC] for i in range(T)]
        xT = [sb(f"xT{i}", [P, ND, P]) for i in range(2)]
        assert U * HT == T and 4 * HT * D == T * D
        xg = [xext[:, u * HT:(u + 1) * HT, :] for u in range(U)]
        y1 = [xb[0][:, i * HT:(i + 1) * HT, :] for i in range(2)]
        y2 = [xb[0][:, (2 + i) * HT:(3 + i) * HT, :] for i in range(2)]
        st = sb("st", [P, T, 6])
        mv = sb("mv", [P, T, 2])
        vv = sb("vv", [P, T])
        rs = sb("rs", [P, T])
        nms = sb("nms", [P, T])
        prT = [sb(f"prT{i}", [P, P]) for i in range(2)]
        psum_p = sb("psum_p", [P, T])
        rsum = sb("rsum", [P, T])
        lg = sb("lg", [P, T, E])
        lgd = sb("lgd", [P, T, E])
        ex = sb("ex", [P, T, E])
        mx = sb("mx", [P, T, 8])
        ix = sb("ix", [P, T, 8], U32)
        ixf = sb("ixf", [P, KO, T])
        oh = sb("oh", [P, KO, T, E])
        msk = sb("msk", [P, T, E])
        msk16 = sb("msk16", [P, T, E], F16)
        gs = sb("gs", [P, T])
        gr = sb("gr", [P, T])
        ge = sb("ge", [P, T, E])
        macc = sb("macc", [P, E], F16)
        msum = sb("msum", [P, E])
        ohp = sb("ohp", [P, KO * T, E])
        lp = sb("lp", [P, KO * T])
        lpi = sb("lpi", [P, KO * T], I32)
        ri = sb("ri", [P, KO * T], I32)
        ji = sb("ji", [P, KO * T], I32)
        rf = sb("rf", [P, KO * T])
        jf = sb("jf", [P, KO * T])
        cf = sb("cf", [P, KO * T])
        Roh = [sb(f"Roh{i}", [P, P], F16) for i in range(2)]
        Joh = [sb(f"Joh{i}", [P, E * JE], F16) for i in range(2)]

        ssq = sb("ssq", [P, 4])
        tick = sb("tick", [P, 1])
        bsq = sb("bsq", [P, NH])
        nrm = sb("nrm", [P, 3])
        bnd = sb("bnd", [P, 2])
        bnd2 = sb("bnd2", [P, 2], I32)
        sclr = sb("sclr", [P, 2])
        scl = sb("scl", [P, 2])
        gg = sb("gg", [P, 1])
        b1raw = sb("b1raw", [P, E * NH])

        nti = sb("nti", [P, E], I32)
        ntj = sb("ntj", [P, E], I32)
        ntf = sb("ntf", [P, E])
        assert off[0] <= 2 * RAW
        off[0] = list_off
        cum = carve(E * E).rearrange("p (f e) -> p f e", f=E)
        endf = sb("endf", [P, E])
        begf = sb("begf", [P, E])
        pick = carve(2 * NBLK * E).rearrange("p (j k e) -> p j k e", j=2, k=NBLK)
        picked = sb("picked", [P, 2, NBLK])
        tgt = sb("tgt", [P, NBLK])
        bad = sb("bad", [P, NBLK])
        tgv = sb("tgv", [P, NBLK])
        LTT = carve(NBLK * P, F16).rearrange("p (k r) -> p k r", k=NBLK)
        Sel = carve(NBLK * SP, F16).rearrange("p (k s) -> p k s", k=NBLK)
        v0 = carve(SP)
        vneg = carve(SP)
        vzero = carve(SP)
        v1 = carve(SP)
        v2 = carve(SP)
        ecmp = carve(SP * E)[0:1, :].rearrange("p (s e) -> p s e", s=SP)
        esum = carve(SP)[0:1, :]
        ecl = carve(SP)[0:1, :]

        assert off[0] <= 2 * RAW

        s_const = sem("s_const")
        s_zrow = sem("s_zrow")
        s_zst = sem("s_zst")
        s_final = sem("s_final")
        s_small = sem("s_small")
        s_ctx = sem("s_ctx")
        s_w = sem("s_w")
        s_x = sem("s_x")
        s_b1 = sem("s_b1")
        s_b1T = sem("s_b1T")
        s_b1c = sem("s_b1c")
        s_b1k = sem("s_b1k")
        s_tanh = sem("s_tanh")
        s_ln1 = sem("s_ln1")
        s_cst2 = sem("s_cst2")
        s_cst3 = sem("s_cst3")
        s_st2 = sem("s_st2")
        s_mv2 = sem("s_mv2")
        s_rs2 = sem("s_rs2")
        s_x2 = sem("s_x2")
        s_x2g = sem("s_x2g")
        s_x2b = sem("s_x2b")
        s_x2T = sem("s_x2T")
        s_x2Tc = sem("s_x2Tc")
        s_wqT = sem("s_wqT")
        s_wqTc = sem("s_wqTc")
        s_kt = sem("s_kt")
        s_ktc = sem("s_ktc")
        s_vt = sem("s_vt")
        s_vtc = sem("s_vtc")
        s_u = sem("s_u")
        s_uc = sem("s_uc")
        s_kq = sem("s_kq")
        s_kqc = sem("s_kqc")
        s_cp = sem("s_cp")
        s_cc = sem("s_cc")
        s_vo = sem("s_vo")
        s_voc = sem("s_voc")
        s_vob = sem("s_vob")
        s_st = sem("s_st")
        s_mv = sem("s_mv")
        s_vv = sem("s_vv")
        s_rs = sem("s_rs")
        s_nm = sem("s_nm")
        s_xhat = sem("s_xhat")
        s_t1 = sem("s_t1")
        s_xT = sem("s_xT")
        s_sc = sem("s_sc")
        s_pr = sem("s_pr")
        s_p2 = sem("s_p2")
        s_prT = sem("s_prT")
        s_rsum = sem("s_rsum")
        s_o = sem("s_o")
        s_x1 = sem("s_x1")
        s_st3 = sem("s_st3")
        s_mv3 = sem("s_mv3")
        s_vv3 = sem("s_vv3")
        s_rs3 = sem("s_rs3")
        s_xn = sem("s_xn")
        s_t2 = sem("s_t2")
        s_xnT = sem("s_xnT")
        s_lg = sem("s_lg")
        s_lgb = sem("s_lgb")
        s_mx8 = sem("s_mx8")
        s_ix = sem("s_ix")
        s_ixf = sem("s_ixf")
        s_lgd = sem("s_lgd")
        s_ex = sem("s_ex")
        s_oh = sem("s_oh")
        s_msk = sem("s_msk")
        s_m16 = sem("s_m16")
        s_gs = sem("s_gs")
        s_gr = sem("s_gr")
        s_gtg = sem("s_gtg")
        s_ge = sem("s_ge")
        s_gx = sem("s_gx")
        s_outd = sem("s_outd")
        s_xrd = sem("s_xrd")
        s_pos = sem("s_pos")
        s_ohp = sem("s_ohp")
        s_lp = sem("s_lp")
        s_lpi = sem("s_lpi")
        s_ri = sem("s_ri")
        s_ji = sem("s_ji")
        s_rf = sem("s_rf")
        s_cf = sem("s_cf")
        s_msum = sem("s_msum")
        s_macc = sem("s_macc")
        s_R = sem("s_R")
        s_inv = sem("s_inv")
        s_ltt = sem("s_ltt")
        s_ssq = sem("s_ssq")
        s_nrm = sem("s_nrm")
        s_nrmc = sem("s_nrmc")
        s_bnd = sem("s_bnd")
        s_bnd2 = sem("s_bnd2")
        s_msb = sem("s_msb")
        s_sclr = sem("s_sclr")
        s_scl = sem("s_scl")
        s_hi1 = sem("s_hi1")
        s_lo = sem("s_lo")
        s_gg = sem("s_gg")
        s_inve = sem("s_inve")
        s_b1e = sem("s_b1e")
        s_b2e = sem("s_b2e")
        s_pow = sem("s_pow")
        s_cnt = sem("s_cnt")
        s_r1 = sem("s_r1")
        s_r2 = sem("s_r2")
        s_r3 = sem("s_r3")
        s_r4 = sem("s_r4")
        s_r5 = sem("s_r5")
        s_r6 = sem("s_r6")
        s_r7 = sem("s_r7")
        s_r8 = sem("s_r8")
        s_ltc = sem("s_ltc")
        s_idp = sem("s_idp")
        s_i1 = sem("s_i1")
        s_pn = sem("s_pn")
        s_i2 = sem("s_i2")
        s_i3 = sem("s_i3")
        s_i4 = sem("s_i4")
        s_idx = sem("s_idx")
        s_e1 = sem("s_e1")
        s_e2 = sem("s_e2")
        s_e3 = sem("s_e3")
        s_eid = sem("s_eid")
        g_ix = sem("g_ix")
        g_ix2 = sem("g_ix2")
        g_T = sem("g_T")
        g_xh = sem("g_xh")
        g_xl = sem("g_xl")
        g_mm1 = sem("g_mm1")
        g_hb = sem("g_hb")
        g_hh = sem("g_hh")
        g_hl = sem("g_hl")
        g_mm2 = sem("g_mm2")
        g_turn = sem("g_turn")
        g_y1 = sem("g_y1")
        g_q = sem("g_q")
        g_y2 = sem("g_y2")
        g_out = sem("g_out")
        s_raw = [sem(f"s_raw{k}") for k in range(EB)]
        g_xg = [sem(f"g_xg{u}") for u in range(U)]

        def tile_tokens(ap, b):
            return ap[ds(b * L, L), :].rearrange("(p i) d -> p i d", p=P)

        x_rows = x.rearrange("b l d -> (b l) d")
        out_rows = out.rearrange("b l d -> (b l) d")
        w1_v = w1.rearrange("e (c p) h -> p (e c) h", p=P)
        w2_v = w2.rearrange("e (c p) d -> p (e c) d", p=P)

        def some(count):
            return not (isinstance(count, int) and count <= 0)

        def turn_of(s, u, i):
            return s // U if isinstance(s, int) else i + u // U

        block = ctx.enter_context(nc.Block())

        @block.sync
        def _(sp):
            def row(ap, n):
                return ap.rearrange("(a n) -> a n", a=1).to_broadcast([P, n])

            sp.dma_start(xb[0][:], tile_tokens(x_rows, 0)).then_inc(s_x, 16)
            sp.dma_start(ctx_s[0:LC, :, :], ctx_768.rearrange("b l d -> l b d")).then_inc(s_ctx, 16)
            sp.dma_start(ln2r[:, 0, :], row(ln2_g, DC)).then_inc(s_ctx, 16)
            sp.dma_start(ln2r[:, 1, :], row(ln2_b, DC)).then_inc(s_ctx, 16)
            for j, g in enumerate((g_xattn, g_ffn)):
                sp.dma_start(gates_in[:, j:j + 1], row(g, 1)).then_inc(s_small, 16)
            sp.dma_start(bor, row(bo, D)).then_inc(s_small, 16)
            sp.dma_start(gbr[:], row(gate_b, E)).then_inc(s_small, 16)
            with nc.allow_non_contiguous_dma(reason="columns of small vectors"):
                for dst, src in ((ln1c[:, 0:ND], ln1_g), (ln1c[:, ND:2 * ND], ln1_b), (bqc[:], bq),
                                 (bkc[:], bk), (bvc[:], bv)):
                    sp.dma_start(dst, src.rearrange("(c p) -> p c", p=P)).then_inc(s_small, 16)
            for dst, src in ((Wk_s, Wk), (Wv_s, Wv)):
                sp.dma_start(dst[:, 0, :], src[0:P, :]).then_inc(s_w, 16)
                sp.dma_start(dst[0:DC2, 1, :], src[P:DC, :]).then_inc(s_w, 16)
            for dst, src in ((Wq_s, Wq), (Wo_s, Wo), (gw_s, gate_w)):
                sp.dma_start(dst[:], src.rearrange("(c p) n -> p c n", p=P)).then_inc(s_w, 16)
            sp.dma_start(b1row, b1.rearrange("e (c p) -> (e c) p", p=P)).then_inc(s_b1, 16)

            def load_x(b):
                sp.dma_start(xb[0][:], tile_tokens(x_rows, b)).then_inc(s_x, 16)

            def load_expert(b, k):
                sp.dma_start(raw[k][:, 0:ND * H].rearrange("p (c h) -> p c h", c=ND),
                             w1_v[:, ds((b * EB + k) * ND, ND), :]).then_inc(s_raw[k], 16)
                sp.dma_start(raw[k][:, ND * H:].rearrange("p (c h) -> p c h", c=NH),
                             w2_v[:, ds((b * EB + k) * NH, NH), :]).then_inc(s_raw[k], 16)
                sp.dma_start(b2s[:, ds((b * EB + k) * D, D)],
                             b2[ds(b * EB + k, 1), :].to_broadcast([P, D])).then_inc(s_raw[k], 16)

            def store_x1(b):
                sp.wait_ge(s_x1, (b + 1) * T)
                sp.dma_start(tile_tokens(sums, b), xb[0][:]).then_inc(s_outd, 16)

            def store_rows(b):
                sp.wait_ge(s_gx, b + 1)
                sp.dma_start(tile_tokens(xrows, b), xext[:]).then_inc(s_xrd, 16)

            sp.wait_ge(s_zrow, 1)
            sp.dma_start(xrows[B * L:B * L + P, :], xext[:, 0, :]).then_inc(s_zst, 16)
            sp.dma_start(sums[B * L:B * L + P, :], xext[:, 0, 0:D]).then_inc(s_zst, 16)
            load_expert(0, 0)
            load_expert(0, 1)
            def next_batch(b):
                store_x1(b)
                sp.wait_ge(s_lo, 2 * b + 1)
                load_expert(b + 1, 0)
                sp.wait_ge(s_outd, (b + 1) * 16)
                sp.wait_ge(s_xn, (b + 1) * T)
                load_x(b + 1)
                store_rows(b)
                sp.wait_ge(s_lo, 2 * b + 2)
                load_expert(b + 1, 1)

            next_batch(0)
            with sp.Fori(1, B - 1) as b:
                next_batch(b)

            store_x1(B - 1)
            store_rows(B - 1)
            sp.wait_ge(g_out, S * HT * 16)
            for b in range(B):
                sp.dma_start(out_rows[b * L:(b + 1) * L, :].rearrange("(p r) d -> p (r d)", p=P),
                             sums[b * L:(b + 1) * L, :].rearrange("(p r) d -> p (r d)", p=P)).then_inc(s_final, 16)
            sp.wait_ge(s_final, B * 16)
            sp.wait_ge(s_outd, B * 16)
            sp.wait_ge(s_xrd, B * 16)

        @block.gpsimd
        def _(pool):
            g = nc.gpsimd
            g.memset(xext[:, 0, :], 0.0).then_inc(s_zrow, 1)
            g.memset(ident[:], 0.0).then_inc(s_const, 1)
            g.memset(ones[:], 1.0).then_inc(s_const, 1)
            g.memset(incl[:], 1.0).then_inc(s_const, 1)
            g.memset(own_e[:], 1.0).then_inc(s_const, 1)
            g.memset(ones16[:], 1.0).then_inc(s_const, 1)
            g.memset(zero16[:], 0.0).then_inc(s_const, 1)
            g.memset(neghalf[:], -0.5).then_inc(s_const, 1)
            g.memset(half[:], 0.5).then_inc(s_const, 1)
            g.memset(macc[:], 0.0).then_inc(s_const, 1)
            g.iota(iotaR[:], [[1, P]], base=0, channel_multiplier=0,
                   allow_small_or_imprecise_dtypes=True).then_inc(s_const, 1)
            g.iota(iotaJ[:], [[1, E * JE]], base=0, channel_multiplier=0,
                   allow_small_or_imprecise_dtypes=True).then_inc(s_const, 1)
            g.iota(iota_e[:], [[1, E]], base=0, channel_multiplier=0,
                   allow_small_or_imprecise_dtypes=True).then_inc(s_const, 1)
            g.iota(iota_s[:], [[1, SP]], base=0, channel_multiplier=0,
                   allow_small_or_imprecise_dtypes=True).then_inc(s_const, 1)
            hb_ = B // 2
            g.iota(tokv[:, 0:hb_ * T], [[L, hb_], [1, T]], base=-B * L // 2, channel_multiplier=T,
                   allow_small_or_imprecise_dtypes=True).then_inc(s_const, 1)
            g.iota(tokv[:, hb_ * T:], [[L, hb_], [1, T]], base=1, channel_multiplier=T,
                   allow_small_or_imprecise_dtypes=True).then_inc(s_const, 1)
            g.iota(jpos_i[:], [[0, 1]], base=0, channel_multiplier=1).then_inc(s_const, 1)
            pool.wait_ge(s_const, 16)
            g.affine_select(out=ident[:], in_=ident[:], compare_op=ALU.not_equal, fill=1.0, base=0,
                            pattern=[[-1, P]], channel_multiplier=1).then_inc(s_cst2, 1)
            g.affine_select(out=before16[:], in_=ones16[:], compare_op=ALU.is_ge, fill=0.0, base=-1,
                            pattern=[[1, P]], channel_multiplier=-1).then_inc(s_cst2, 1)
            g.affine_select(out=incl[:], in_=incl[:], compare_op=ALU.is_ge, fill=0.0, base=0,
                            pattern=[[1, E], [-1, E]], channel_multiplier=0).then_inc(s_cst2, 1)
            g.affine_select(out=own_e[:], in_=own_e[:], compare_op=ALU.is_ge, fill=0.0, base=0,
                            pattern=[[P, NBLK], [-JE, E]], channel_multiplier=1).then_inc(s_cst2, 1)
            pool.wait_ge(s_cst2, 4)
            g.affine_select(out=own_e[:], in_=own_e[:], compare_op=ALU.is_ge, fill=0.0, base=JE - 1,
                            pattern=[[-P, NBLK], [JE, E]], channel_multiplier=-1).then_inc(s_cst3, 1)
            pool.wait_ge(s_mv2, 2)
            g.tensor_tensor(rs2[0:LC, :], rs2[0:LC, :], neghalf[0:LC, 0:B], ALU.pow).then_inc(s_rs2, 1)

            def root(b, k):
                pool.wait_ge(s_nrmc, b * EB + k + 1)
                g.tensor_tensor(nrm[:], nrm[:], half[:, 0:1].to_broadcast([P, 3]), ALU.pow).then_inc(s_pow, 1)

            def norms(b):
                pool.wait_ge(s_vv, b + 1)
                if some(b * T):
                    pool.wait_ge(s_xhat, b * T)
                g.tensor_tensor(rs[:], vv[:], neghalf[:], ALU.pow).then_inc(s_rs, 1)
                root(b, 0)
                pool.wait_ge(s_vv3, b + 1)
                g.tensor_tensor(rs[:], vv[:], neghalf[:], ALU.pow).then_inc(s_rs3, 1)
                root(b, 1)

            norms(0)
            with pool.Fori(1, B) as b:
                norms(b)

            pool.wait_ge(s_idx, 1)
            pool.wait_ge(s_xrd, B * 16)
            pool.wait_ge(s_outd, B * 16)
            pool.wait_ge(s_zst, 32)

            def gather(s, u):
                for h in range(HT):
                    g.tensor_copy(idx[u * HT + h][:], idx_tab[:, ds(s * HT + h, 1)]).then_inc(g_ix, 1)
                pool.wait_ge(g_ix, (s + 1) * HT)
                pool.sem_inc(g_turn)
                for h in range(HT):
                    g.indirect_dma_start(out=xg[u][:, h, :], out_offset=None, in_=xrows,
                                         in_offset=bass.IndirectOffsetOnAxis(ap=idx[u * HT + h][:, 0:1], axis=0)
                                         ).then_inc(g_xg[u], 16)

            def scatter(s, u):
                at = [idx_out[u % 2 * HT + h] for h in range(HT)]
                for h in range(HT):
                    g.tensor_copy(at[h][:], idx_tab[:, ds(s * HT + h, 1)]).then_inc(g_ix2, 1)
                pool.wait_ge(g_ix2, (s + 1) * HT)
                pool.wait_ge(g_y2, s + 1)
                for h in range(HT):
                    if some(s * HT + h):
                        pool.wait_ge(g_out, (s * HT + h) * 16)
                    pool.sem_inc(g_turn)
                    g.indirect_dma_start(out=sums, out_offset=bass.IndirectOffsetOnAxis(ap=at[h][:, 0:1], axis=0),
                                         in_=y2[u % 2][:, h, :], in_offset=None, compute_op=ALU.add).then_inc(g_out, 16)

            for s in range(U):
                gather(s, s)

            def step(s, u, i=None, last=False):
                if not last:
                    pool.wait_ge(g_T, s + 1)
                    pool.wait_ge(g_q, s + 1)
                    gather(s + U, u)
                if some(s - 1):
                    pool.wait_ge(g_out, (s - 1) * HT * 16)
                scatter(s, u)

            for s in range(U):
                step(s, s)
            with pool.Fori(1, LOOPS) as i:
                for u in range(U):
                    step(i * U + u, u, i)
            for s in range(LOOPS * U, S):
                step(s, s % U, last=s + U >= S)
            pool.wait_ge(g_out, S * HT * 16)

        @block.scalar
        def _(act):
            a = nc.scalar
            act.wait_ge(s_small, 16 * 9)
            a.activation(tg[:], gates_in[:], ACT.Tanh).then_inc(s_tanh, 1)
            a.mul(ln1s[:], ln1c[:, 0:ND], SCALE).then_inc(s_ln1, 1)
            act.wait_ge(s_ln1, 1)
            for b in range(B):
                act.wait_ge(s_x2T, b + 1)
                a.copy(x2T[0][:, b * LC:(b + 1) * LC], bank[b % 4][:, 0:LC])
                a.copy(x2T[1][0:DC2, b * LC:(b + 1) * LC], bank[b % 4][0:DC2, P:P + LC]).then_inc(s_x2Tc, 1)
            for c in range(ND):
                act.wait_ge(s_wqT, c + 1)
                a.copy(WqT[:, c, :], bank[4 + c][:, 0:D]).then_inc(s_wqTc, 1)
            for c in range(ND):
                act.wait_ge(s_kt, c + 1)
                a.activation(KT[c], bank[c][:, 0:NC], ACT.Identity, bias=bkc[:, c:c + 1]).then_inc(s_ktc, 1)
            for c in range(ND):
                act.wait_ge(s_vt, c + 1)
                a.activation(VT[c], bank[2 + c][:, 0:NC], ACT.Identity, bias=bvc[:, c:c + 1]).then_inc(s_vtc, 1)
            for c in range(ND):
                act.wait_ge(s_kq, c + 1)
                a.activation(KQ[c][:], bank[4 + c][:, 0:NC], ACT.Copy, scale=ln1s[:, c:c + 1]).then_inc(s_kqc, 1)
            act.wait_ge(s_cp, 1)
            a.mul(cst[:], bank[6][0:1, 0:NC], SCALE).then_inc(s_cc, 1)
            act.wait_ge(s_b1T, 1)
            a.copy(b1raw[:], bank[7][:, 0:E * NH]).then_inc(s_b1c, 1)

            def squares(b, k):
                act.wait_ge(s_raw[k], (b + 1) * 48)
                if some(b * EB + k):
                    act.wait_ge(s_nrm, b * EB + k)
                if k == 0:
                    act.wait_ge(s_b1k, 1)
                for j, junk in enumerate((w1l, w2l)):
                    src = raw[k][:, j * ND * H:(j + 1) * ND * H]
                    a.activation(junk[:, ds((b * EB + k) * ND * H, ND * H)], src, ACT.Square, accum_out=ssq[:, j:j + 1])
                a.activation(bsq[:], b1raw[:, ds((b * EB + k) * NH, NH)], ACT.Square,
                             accum_out=ssq[:, 2:3]).then_inc(s_ssq, 1)

            def hi_parts(b, k):
                act.wait_ge(s_scl, b * EB + k + 1)
                a.activation(w1h[:, ds((b * EB + k) * ND * H, ND * H)], raw[k][:, 0:ND * H], ACT.Copy,
                             scale=scl[:, 0:1]).then_inc(s_hi1, 1)
                a.activation(w2h[:, ds((b * EB + k) * NH * D, NH * D)], raw[k][:, ND * H:], ACT.Copy,
                             scale=scl[:, 1:2]).then_inc(s_hi1, 1)

            def softmax_exp(b, i):
                act.wait_ge(s_nm, b * T + i + 1)
                if some(b * T):
                    act.wait_ge(s_p2, b * T)
                a.activation(pr[i], bank[2 + i % 2][:, 0:LC], ACT.Exp, bias=nms[:, i:i + 1],
                             accum_out=psum_p[:, i:i + 1]).then_inc(s_pr, 1)

            def batch(b):
                squares(b, 0)
                for i in range(T):
                    act.wait_ge(s_t1, b * T + i + 1)
                    if i >= 2:
                        act.wait_ge(s_sc, b * T + i - 1)
                    else:
                        if some(b * T):
                            act.wait_ge(s_lg, b * T)
                    a.copy(xT[i % 2][:], bank[i % 2][:, 0:ND * P].rearrange("p (c t) -> p c t", c=ND)).then_inc(s_xT, 1)
                    if i >= 2:
                        softmax_exp(b, i - 2)
                softmax_exp(b, T - 2)
                softmax_exp(b, T - 1)
                hi_parts(b, 0)
                squares(b, 1)
                for i in range(T):
                    act.wait_ge(s_t2, b * T + i + 1)
                    if i >= 2:
                        act.wait_ge(s_lg, b * T + i - 1)
                    a.copy(xT[i % 2][:], bank[i % 2][:, 0:ND * P].rearrange("p (c t) -> p c t", c=ND)).then_inc(s_xnT, 1)
                act.wait_ge(s_lgd, b + 1)
                a.activation(ex[:], lgd[:], ACT.Exp).then_inc(s_ex, 1)
                hi_parts(b, 1)

            batch(0)
            with act.Fori(1, B) as b:
                batch(b)

            act.wait_ge(s_lo, 2 * B)

            def x_hi(s, u):
                act.wait_ge(g_T, s + 1)
                if some(NHB * (s - 1)):
                    act.wait_ge(g_mm1, NHB * (s - 1))
                a.copy(xh[u % 2], bank[6 + u % 2][:, 0:ND * PS]).then_inc(g_xh, 1)

            def h_hi(s, u):
                for j in range(NHB):
                    act.wait_ge(g_hb, NHB * s + j + 1)
                    if some(s - 1):
                        act.wait_ge(g_mm2, s - 1)
                    a.activation(hh[u % 2][:, j * 512:(j + 1) * 512], hb[j], ACT.Relu).then_inc(g_hh, 1)

            def y_scale(s, u):
                act.wait_ge(g_y1, s + 1)
                act.wait_ge(g_q, s + 1)
                if some((s - 1) * HT * 16):
                    act.wait_ge(g_out, (s - 1) * HT * 16)
                for h in range(HT):
                    ins = a.activation(y2[u % 2][:, h, :], y1[u % 2][:, h, :], ACT.Copy, scale=q[u % U][:, h:h + 1])
                ins.then_inc(g_y2, 1)

            x_hi(0, 0)
            x_hi(1, 1)
            h_hi(0, 0)

            def step(s, u, i=None):
                if not (isinstance(s, int) and s + 2 >= S):
                    x_hi(s + 2, u)
                if not (isinstance(s, int) and s + 1 >= S):
                    h_hi(s + 1, u + 1)
                y_scale(s, u)

            step(0, 0)
            step(1, 1)
            step(2, 2)
            step(3, 3)
            with act.Fori(1, LOOPS) as i:
                for u in range(U):
                    step(i * U + u, u, i)
            for s in range(LOOPS * U, S):
                step(s, s % U)

        @block.vector
        def _(dve):
            v = nc.vector
            dve.wait_ge(s_ctx, 48)
            for b in range(B):
                v.bn_stats(st2[0:LC, b, :], ctx_s[0:LC, b, :]).then_inc(s_st2, 1)
            dve.wait_ge(s_st2, B)
            for b in range(B):
                ins = v.bn_aggr(mv2[0:LC, b, :], st2[0:LC, b, :])
            ins.then_inc(s_mv2, 1)
            dve.wait_ge(s_mv2, 1)
            dve.wait_ge(s_const, 16)
            v.tensor_scalar(rs2[0:LC, :], mv2[0:LC, :, 1], EPS, None, ALU.add).then_inc(s_mv2, 1)
            dve.wait_ge(s_rs2, 1)
            for b in range(B):
                v.tensor_scalar(ctx_s[0:LC, b, :], ctx_s[0:LC, b, :], mv2[0:LC, b, 0:1], rs2[0:LC, b:b + 1],
                                ALU.subtract, ALU.mult).then_inc(s_x2, 1)
            dve.wait_ge(s_x2, B)
            v.tensor_tensor(ctx_s[0:LC, :, :], ctx_s[0:LC, :, :],
                            ln2r[0:LC, 0:1, :].to_broadcast([LC, B, DC]), ALU.mult).then_inc(s_x2g, 1)
            dve.wait_ge(s_x2g, 1)
            v.tensor_tensor(ctx_s[0:LC, :, :], ctx_s[0:LC, :, :],
                            ln2r[0:LC, 1:2, :].to_broadcast([LC, B, DC]), ALU.add).then_inc(s_x2b, 1)
            v.tensor_copy(pnum[:], jpos_i[:]).then_inc(s_pn, 1)
            dve.wait_ge(s_pn, 1)
            v.tensor_scalar(empty[:], pnum[:], float(B * L // 2 + 1), None, ALU.add).then_inc(s_pn, 1)
            v.tensor_scalar(jpos_i[:], jpos_i[:], JE - 1, None, ALU.bitwise_and).then_inc(s_i1, 1)
            dve.wait_ge(s_i1, 1)
            v.tensor_copy(jpos[:], jpos_i[:]).then_inc(s_i1, 1)
            dve.wait_ge(s_small, 16 * 9)
            dve.wait_ge(s_u, 1)
            v.tensor_tensor(uq[:], bank[7][:, 0:ND], bqc[:], ALU.add).then_inc(s_uc, 1)
            dve.wait_ge(s_tanh, 1)
            for b in range(B):
                dve.wait_ge(s_vo, b + 1)
                v.tensor_tensor(VO[0:LC, b * D:(b + 1) * D], bank[b % 2][0:LC, 0:D], bor[0:LC, :], ALU.add).then_inc(s_voc, 1)
            dve.wait_ge(s_voc, B)
            v.tensor_scalar(VO[0:LC, :], VO[0:LC, :], tg[0:LC, 0:1], None, ALU.mult).then_inc(s_vob, 1)
            dve.wait_ge(s_b1c, 1)
            v.tensor_copy(b1s[:], b1raw[:]).then_inc(s_b1k, 1)

            def scales(b, k):
                e = b * EB + k
                dve.wait_ge(s_nrm, e + 1)
                if some(2 * e):
                    dve.wait_ge(s_bnd, 2 * e)
                v.tensor_copy(nrm[:], bank[5][:, 0:3]).then_inc(s_nrmc, 1)
                dve.wait_ge(s_pow, e + 1)
                v.scalar_tensor_tensor(bnd[:, 0:1], nrm[:, 0:1], float(D) ** 0.5, nrm[:, 2:3], ALU.mult,
                                       ALU.add).then_inc(s_bnd, 1)
                v.tensor_copy(bnd[:, 1:2], nrm[:, 1:2]).then_inc(s_bnd, 1)
                dve.wait_ge(s_bnd, 2 * e + 2)
                v.tensor_scalar(sclr[:], bnd[:], 1e-15, None, ALU.max).then_inc(s_bnd2, 1)
                dve.wait_ge(s_bnd2, e + 1)
                v.tensor_scalar(bnd2[:], sclr[:].bitcast(I32), 0x7F800000, None, ALU.bitwise_and).then_inc(s_msb, 1)
                dve.wait_ge(s_msb, e + 1)
                v.reciprocal(sclr[:], bnd2[:].bitcast(F32)).then_inc(s_sclr, 1)
                dve.wait_ge(s_sclr, e + 1)
                if some(2 * e):
                    dve.wait_ge(s_hi1, 2 * e)
                v.tensor_scalar(scl[:, 0:1], sclr[:, 0:1], 2.0 ** 14, None, ALU.mult)
                v.tensor_scalar(scl[:, 1:2], sclr[:, 1:2], 2.0 ** 13, None, ALU.mult).then_inc(s_scl, 1)

            def lo_parts(b, k):
                e = b * EB + k
                dve.wait_ge(s_scl, e + 1)
                v.tensor_tensor(gg[:], scl[:, 0:1], scl[:, 1:2], ALU.mult).then_inc(s_gg, 1)
                v.tensor_scalar(b1s[:, ds(e * NH, NH)], b1s[:, ds(e * NH, NH)], scl[:, 0:1], None, ALU.mult).then_inc(s_b1e, 1)
                dve.wait_ge(s_gg, e + 1)
                v.reciprocal(inv[:, ds(e, 1)], gg[:]).then_inc(s_inve, 1)
                v.tensor_scalar(b2s[:, ds(e * D, D)], b2s[:, ds(e * D, D)], gg[:], None, ALU.mult).then_inc(s_b2e, 1)
                for j, (wh, wl, n) in enumerate(((w1h, w1l, ND * H), (w2h, w2l, NH * D))):
                    dve.wait_ge(s_hi1, 2 * e + j + 1)
                    ins = v.scalar_tensor_tensor(wl[:, ds(e * n, n)], raw[k][:, j * n:(j + 1) * n], scl[:, j:j + 1],
                                                 wh[:, ds(e * n, n)], ALU.mult, ALU.subtract)
                ins.then_inc(s_lo, 1)

            def one_hots(b, n):
                if n >= 2:
                    dve.wait_ge(s_inv, b * KO * T + n - 1)
                v.tensor_scalar(Roh[n % 2][:], iotaR[:], rf[:, n:n + 1], None, ALU.is_equal)
                v.tensor_scalar(Joh[n % 2][:], iotaJ[:], cf[:, n:n + 1], tokv[:, ds(b * T + n % T, 1)],
                                ALU.is_equal, ALU.mult).then_inc(s_R, 1)

            def row_max(b, i):
                dve.wait_ge(s_sc, b * T + i + 1)
                v.tensor_reduce(nms[:, i:i + 1], bank[2 + i % 2][:, 0:LC], AX.X, ALU.max, negate=True).then_inc(s_nm, 1)

            def residual(b, i):
                dve.wait_ge(s_o, b * T + i + 1)
                v.scalar_tensor_tensor(xb[0][:, i, :], bank[2 + i % 2][:, 0:D], rsum[:, i:i + 1], xb[0][:, i, :],
                                       ALU.mult, ALU.add).then_inc(s_x1, 1)

            def batch(b):
                last = None if isinstance(b, int) else b - 1
                dve.wait_ge(s_x, (b + 1) * 16)
                for i in range(T):
                    v.bn_stats(st[:, i, :], xb[0][:, i, :]).then_inc(s_st, 1)
                dve.wait_ge(s_st, (b + 1) * T)
                v.memset(tick[:], 0)
                for i in range(T):
                    v.bn_aggr(mv[:, i, :], st[:, i, :]).then_inc(s_mv, 1)
                dve.wait_ge(s_mv, (b + 1) * T)
                v.tensor_scalar(vv[:], mv[:, :, 1], 1.0 + EPS, EPS * EPS, ALU.mult, ALU.add).then_inc(s_vv, 1)
                if last is not None:
                    lo_parts(last, 1)
                dve.wait_ge(s_rs, b + 1)
                for i in range(T):
                    if i == 0:
                        dve.wait_ge(s_zst, 32)
                        if some(b * 16):
                            dve.wait_ge(s_xrd, b * 16)
                    v.tensor_scalar(xhat[i], xb[0][:, i, :], mv[:, i, 0:1], rs[:, i:i + 1], ALU.subtract,
                                    ALU.mult).then_inc(s_xhat, 1)
                    if last is not None:
                        one_hots(last, 2 * i)
                        one_hots(last, 2 * i + 1)
                    if i >= 2:
                        row_max(b, i - 2)
                row_max(b, T - 2)
                row_max(b, T - 1)
                scales(b, 0)
                dve.wait_ge(s_pr, (b + 1) * T)
                v.reciprocal(rsum[:], psum_p[:]).then_inc(s_rsum, 1)
                dve.wait_ge(s_rsum, b + 1)
                for i in range(T):
                    dve.wait_ge(s_p2, b * T + i + 1)
                    if i >= 2:
                        dve.wait_ge(s_o, b * T + i - 1)
                    v.tensor_copy(prT[i % 2][0:LC, :], bank[i % 2][0:LC, 0:P]).then_inc(s_prT, 1)
                    if i >= 1:
                        residual(b, i - 1)
                residual(b, T - 1)
                dve.wait_ge(s_x1, (b + 1) * T)
                for i in range(T):
                    v.bn_stats(st[:, i, :], xb[0][:, i, :]).then_inc(s_st3, 1)
                dve.wait_ge(s_st3, (b + 1) * T)
                v.memset(tick[:], 0)
                for i in range(T):
                    v.bn_aggr(mv[:, i, :], st[:, i, :]).then_inc(s_mv3, 1)
                dve.wait_ge(s_mv3, (b + 1) * T)
                v.tensor_scalar(vv[:], mv[:, :, 1], EPS, None, ALU.add).then_inc(s_vv3, 1)
                dve.wait_ge(s_rs3, b + 1)
                for i in range(T):
                    v.tensor_scalar(xext[:, i, 0:D], xb[0][:, i, :], mv[:, i, 0:1], rs[:, i:i + 1], ALU.subtract,
                                    ALU.mult).then_inc(s_xn, 1)
                lo_parts(b, 0)
                scales(b, 1)
                dve.wait_ge(s_lg, (b + 1) * T)
                v.tensor_tensor(lg[:], bank[4][:, 0:T * E].rearrange("p (t e) -> p t e", t=T),
                                gbr[:].rearrange("p (a e) -> p a e", a=1).to_broadcast([P, T, E]), ALU.add).then_inc(s_lgb, 1)
                dve.wait_ge(s_lgb, b + 1)
                v.memset(tick[:], 0)
                for i in range(T):
                    v.max(mx[:, i, :], lg[:, i, :]).then_inc(s_mx8, 1)
                dve.wait_ge(s_mx8, (b + 1) * T)
                v.memset(tick[:], 0)
                for i in range(T):
                    v.max_index(ix[:, i, :], mx[:, i, :], lg[:, i, :]).then_inc(s_ix, 1)
                v.tensor_tensor(lgd[:], lg[:], mx[:, :, 0:1].to_broadcast([P, T, E]), ALU.subtract).then_inc(s_lgd, 1)
                dve.wait_ge(s_ix, (b + 1) * T)
                v.tensor_copy(ixf[:].rearrange("p k t -> p t k"), ix[:, :, 0:KO]).then_inc(s_ixf, 1)
                dve.wait_ge(s_ixf, b + 1)
                for k in range(KO):
                    v.tensor_tensor(oh[:, k, :, :], iota_e[:].rearrange("p (a e) -> p a e", a=1).to_broadcast([P, T, E]),
                                    ixf[:, k, :].rearrange("p (t a) -> p t a", a=1).to_broadcast([P, T, E]),
                                    ALU.is_equal).then_inc(s_oh, 1)
                dve.wait_ge(s_oh, 2 * (b + 1))
                v.tensor_tensor(msk[:], oh[:, 0, :, :], oh[:, 1, :, :], ALU.add).then_inc(s_msk, 1)
                dve.wait_ge(s_msk, b + 1)
                v.tensor_copy(msk16[:], msk[:]).then_inc(s_m16, 1)
                dve.wait_ge(s_ex, b + 1)
                v.tensor_reduce(gs[:], ex[:], AX.X, ALU.add).then_inc(s_gs, 1)
                v.tensor_tensor(ge[:], ex[:], msk[:], ALU.mult).then_inc(s_ge, 1)
                dve.wait_ge(s_gs, b + 1)
                v.reciprocal(gr[:], gs[:]).then_inc(s_gr, 1)
                dve.wait_ge(s_gr, b + 1)
                v.tensor_scalar(gr[:], gr[:], tg[:, 1:2], None, ALU.mult).then_inc(s_gtg, 1)
                dve.wait_ge(s_gtg, b + 1)
                dve.wait_ge(s_ge, b + 1)
                v.tensor_tensor(xext[:, :, D:XW], ge[:], gr[:].rearrange("p (t a) -> p t a", a=1).to_broadcast([P, T, E]),
                                ALU.mult).then_inc(s_gx, 1)
                dve.wait_ge(s_pos, b + 1)
                for k in range(KO):
                    v.tensor_tensor(ohp[:, k * T:(k + 1) * T, :], oh[:, k, :, :],
                                    bank[4][:, 128:128 + T * E].rearrange("p (t e) -> p t e", t=T), ALU.mult).then_inc(s_ohp, 1)
                dve.wait_ge(s_ohp, 2 * (b + 1))
                v.tensor_reduce(lp[:], ohp[:], AX.X, ALU.add).then_inc(s_lp, 1)
                v.tensor_reduce(msum[:], msk[:].rearrange("p t e -> p e t"), AX.X, ALU.add).then_inc(s_msum, 1)
                dve.wait_ge(s_lp, b + 1)
                v.tensor_copy(lpi[:], lp[:]).then_inc(s_lpi, 1)
                dve.wait_ge(s_msum, b + 1)
                v.tensor_tensor(macc[:], macc[:], msum[:], ALU.add).then_inc(s_macc, 1)
                dve.wait_ge(s_lpi, b + 1)
                v.tensor_scalar(ri[:], lpi[:], P - 1, None, ALU.bitwise_and).then_inc(s_ri, 1)
                v.tensor_scalar(ji[:], lpi[:], 7, None, ALU.arith_shift_right).then_inc(s_ji, 1)
                dve.wait_ge(s_ri, b + 1)
                v.tensor_copy(rf[:], ri[:]).then_inc(s_rf, 1)
                dve.wait_ge(s_ji, b + 1)
                v.tensor_copy(jf[:], ji[:]).then_inc(s_rf, 1)
                dve.wait_ge(s_rf, 2 * (b + 1))
                v.scalar_tensor_tensor(cf[:], ixf[:].rearrange("p k t -> p (k t)"), float(JE), jf[:], ALU.mult,
                                       ALU.add).then_inc(s_cf, 1)
                dve.wait_ge(s_cf, b + 1)

            batch(0)
            with dve.Fori(1, B) as b:
                batch(b)

            for n in range(KO * T):
                one_hots(B - 1, n)
            lo_parts(B - 1, 1)

            dve.wait_ge(s_cnt, 1)
            v.tensor_scalar(ntf[:], bank[5][:, 0:E], float(PS - 1), None, ALU.add).then_inc(s_r1, 1)
            dve.wait_ge(s_r1, 1)
            v.tensor_copy(nti[:], ntf[:]).then_inc(s_r1, 1)
            dve.wait_ge(s_r1, 2)
            v.tensor_scalar(ntj[:], nti[:], PS.bit_length() - 1, HT // 2, ALU.arith_shift_right,
                            ALU.logical_shift_left).then_inc(s_r1, 1)
            dve.wait_ge(s_r1, 3)
            v.tensor_copy(ntf[:], ntj[:]).then_inc(s_r1, 1)
            dve.wait_ge(s_r1, 4)
            v.tensor_tensor(cum, incl[:], ntf[:].rearrange("p (a e) -> p a e", a=1).to_broadcast([P, E, E]),
                            ALU.mult).then_inc(s_r2, 1)
            dve.wait_ge(s_r2, 1)
            v.tensor_reduce(endf[:], cum, AX.X, ALU.add).then_inc(s_r3, 1)
            dve.wait_ge(s_r3, 1)
            v.tensor_tensor(begf[:], endf[:], ntf[:], ALU.subtract).then_inc(s_r4, 1)
            dve.wait_ge(s_r4, 1)
            dve.wait_ge(s_cst3, 1)
            for j, src in enumerate((begf, ntf)):
                v.tensor_tensor(pick[:, j, :, :], own_e[:], src[:].rearrange("p (a e) -> p a e", a=1).to_broadcast(
                    [P, NBLK, E]), ALU.mult).then_inc(s_r5, 1)
            dve.wait_ge(s_r5, 2)
            v.tensor_reduce(picked[:], pick, AX.X, ALU.add).then_inc(s_r6, 1)
            dve.wait_ge(s_r6, 1)
            v.tensor_scalar(tgt[:], picked[:, 0, :], jpos[:, 0:1], None, ALU.add).then_inc(s_r7, 1)
            v.tensor_scalar(bad[:], picked[:, 1, :], jpos[:, 0:1], 1000.0, ALU.is_le, ALU.mult).then_inc(s_r7, 1)
            dve.wait_ge(s_r7, 2)
            v.tensor_tensor(tgv[:], tgt[:], bad[:], ALU.add).then_inc(s_r8, 1)
            dve.wait_ge(s_r8, 1)
            dve.wait_ge(s_ltt, 1)
            for k in range(NBLK):
                v.tensor_scalar(Sel[:, k, :], iota_s[:], tgv[:, k:k + 1], None, ALU.is_equal)
                v.tensor_copy(LTT[:, k, :], bank[6 + k][:, 0:P]).then_inc(s_ltc, 1)
            v.tensor_tensor(ecmp, iota_s[0:1, :].rearrange("p (s a) -> p s a", a=1).to_broadcast([1, SP, E]),
                            endf[0:1, :].rearrange("p (a e) -> p a e", a=1).to_broadcast([1, SP, E]),
                            ALU.is_ge).then_inc(s_e1, 1)
            dve.wait_ge(s_e1, 1)
            v.tensor_reduce(esum, ecmp, AX.X, ALU.add).then_inc(s_e2, 1)
            dve.wait_ge(s_e2, 1)
            v.tensor_scalar(ecl, esum, float(E - 1), None, ALU.min).then_inc(s_e3, 1)
            dve.wait_ge(s_e3, 1)
            v.tensor_copy(eid[:], ecl).then_inc(s_eid, 1)
            dve.wait_ge(s_idp, 1)
            v.tensor_copy(v0, bank[5][:, 128:128 + SP]).then_inc(s_i2, 1)
            dve.wait_ge(s_i2, 1)
            v.tensor_scalar(vneg, v0, 0.0, None, ALU.is_lt).then_inc(s_i3, 1)
            v.tensor_scalar(vzero, v0, 0.0, empty[:, 0:1], ALU.is_equal, ALU.mult).then_inc(s_i3, 1)
            dve.wait_ge(s_i3, 2)
            v.scalar_tensor_tensor(v1, v0, float(B * L // 2 - 1), vneg, ALU.add, ALU.add).then_inc(s_i4, 1)
            dve.wait_ge(s_i4, 1)
            v.tensor_tensor(v2, v1, vzero, ALU.add).then_inc(s_i4, 1)
            dve.wait_ge(s_i4, 2)
            v.tensor_copy(idx_tab[:], v2).then_inc(s_idx, 1)
            dve.wait_ge(s_lo, 2 * B)

            dve.wait_ge(s_eid, 1)
            dve.wait_ge(s_outd, B * 16)

            def x_lo(s, u, i=None):
                e = dve.value_load(eid[0:1, ds(s * HT, 1)], min_val=0, max_val=E - 1)
                if some(s - 3):
                    dve.wait_ge(g_y2, s - 3)
                dve.wait_ge(g_xg[u % U], (turn_of(s, u, i) + 1) * HT * 16)
                v.tensor_tensor(q[u % U][:], xg[u % U][:, :, ds(e + D, 1)].rearrange("p h a -> p (h a)"),
                                inv[:, ds(e, 1)].to_broadcast([P, HT]), ALU.mult).then_inc(g_q, 1)
                dve.wait_ge(g_xh, s + 1)
                v.tensor_tensor(xl[u % 2], bank[6 + u % 2][:, 0:ND * PS], xh[u % 2], ALU.subtract).then_inc(g_xl, 1)

            def h_parts(s, u, first=False):
                e = dve.value_load(eid[0:1, ds(s * HT, 1)], min_val=0, max_val=E - 1)
                pb = u % 2
                for j in range(NHB):
                    dve.wait_ge(g_mm1, NHB * s + j + 1)
                    if not first:
                        dve.wait_ge(g_hl, NHB * (s - 1) + j + 1)
                    v.tensor_tensor(hb[j].rearrange("p (c t) -> p c t", c=HC),
                                    bank[j][:, :].rearrange("p (c t) -> p c t", c=HC),
                                    b1s[:, ds(e * NH + HC * j, HC)].rearrange("p (c a) -> p c a", a=1).to_broadcast([P, HC, PS]),
                                    ALU.add).then_inc(g_hb, 1)
                for j in range(NHB):
                    dve.wait_ge(g_hh, NHB * s + j + 1)
                    v.scalar_tensor_tensor(hl[pb][:, j * 512:(j + 1) * 512], hb[j], 0.0, hh[pb][:, j * 512:(j + 1) * 512],
                                           ALU.max, ALU.subtract).then_inc(g_hl, 1)

            def y_sum(s, u, i=None):
                e = dve.value_load(eid[0:1, ds(s * HT, 1)], min_val=0, max_val=E - 1)
                if some(s - 1):
                    dve.wait_ge(g_y2, s - 1)
                dve.wait_ge(g_mm2, s + 1)
                v.tensor_tensor(y1[u % 2], bank[4 + u % 2][:, :].rearrange("p (h d) -> p h d", h=HT),
                                b2s[:, ds(e * D, D)].rearrange("p (a d) -> p a d", a=1).to_broadcast([P, HT, D]),
                                ALU.add).then_inc(g_y1, 1)

            x_lo(0, 0)
            x_lo(1, 1)
            h_parts(0, 0, first=True)

            def step(s, u, i=None):
                if not (isinstance(s, int) and s + 2 >= S):
                    x_lo(s + 2, u + 2, i)
                if not (isinstance(s, int) and s + 1 >= S):
                    h_parts(s + 1, u + 1)
                y_sum(s, u, i)

            for s in range(U):
                step(s, s)
            with dve.Fori(1, LOOPS) as i:
                for u in range(U):
                    step(i * U + u, u, i)
            for s in range(LOOPS * U, S):
                step(s, s % U)

        @block.tensor
        def _(pe):
            t = nc.tensor
            pe.wait_ge(s_cst2, 4)
            pe.wait_ge(s_w, 16 * 7)
            pe.wait_ge(s_small, 16 * 9)
            for c in range(ND):
                for dc in range(ND):
                    mm = t.matmul(bank[7][:, c:c + 1], Wq_s[:, dc, c * P:(c + 1) * P], ln1c[:, ND + dc:ND + dc + 1],
                                  start=dc == 0, stop=dc == ND - 1)
            mm.then_inc(s_u, 1)
            for c in range(ND):
                for dc in range(ND):
                    mm = t.transpose(bank[4 + c][:, dc * P:(dc + 1) * P], Wq_s[:, dc, c * P:(c + 1) * P], ident[:])
                mm.then_inc(s_wqT, 1)
            pe.wait_ge(s_x2b, 1)
            for b in range(B):
                t.transpose(bank[b % 4][:, 0:LC], ctx_s[0:LC, b, 0:P], ident[0:LC, 0:LC])
                t.transpose(bank[b % 4][0:DC2, P:P + LC], ctx_s[0:LC, b, P:DC], ident[0:LC, 0:LC]).then_inc(s_x2T, 1)
            pe.wait_ge(s_x2Tc, B)
            for dst, W_s, done in ((0, Wk_s, s_kt), (2, Wv_s, s_vt)):
                for c in range(ND):
                    t.matmul(bank[dst + c][:, 0:NC], W_s[:, 0, c * P:(c + 1) * P], x2T[0], start=True, stop=False)
                    t.matmul(bank[dst + c][:, 0:NC], W_s[0:DC2, 1, c * P:(c + 1) * P], x2T[1][0:DC2, :],
                             start=False, stop=True).then_inc(done, 1)
            pe.wait_ge(s_wqTc, ND)
            pe.wait_ge(s_ktc, ND)
            for c in range(ND):
                for ec in range(ND):
                    mm = t.matmul(bank[4 + c][:, 0:NC], WqT[:, ec, c * P:(c + 1) * P], KT[ec], start=ec == 0,
                                  stop=ec == ND - 1)
                mm.then_inc(s_kq, 1)
            pe.wait_ge(s_uc, 1)
            for ec in range(ND):
                mm = t.matmul(bank[6][0:1, 0:NC], uq[:, ec:ec + 1], KT[ec], start=ec == 0, stop=ec == ND - 1)
            mm.then_inc(s_cp, 1)
            pe.wait_ge(s_vtc, ND)
            for b in range(B):
                if b >= 2:
                    pe.wait_ge(s_voc, b - 1)
                for ec in range(ND):
                    mm = t.matmul(bank[b % 2][0:LC, 0:D], VT[ec][:, b * LC:(b + 1) * LC], Wo_s[:, ec, :],
                                  start=ec == 0, stop=ec == ND - 1)
                mm.then_inc(s_vo, 1)
            pe.wait_ge(s_b1, 16)
            t.transpose(bank[7][:, 0:E * NH], b1row, ident[0:E * NH, 0:E * NH]).then_inc(s_b1T, 1)
            pe.wait_ge(s_cc, 1)
            pe.wait_ge(s_b1c, 1)
            for k in range(NBLK):
                t.matmul(bank[6 + k][:, 0:P], zero16[:], zero16[:], start=True, stop=False)
            pe.wait_ge(s_vob, 1)
            pe.wait_ge(s_kqc, ND)

            def norms(b, k):
                e = b * EB + k
                pe.wait_ge(s_ssq, e + 1)
                if some(e):
                    pe.wait_ge(s_nrmc, e)
                t.matmul(bank[5][:, 0:3], ones[:], ssq[:, 0:3], start=True, stop=True).then_inc(s_nrm, 1)

            def invert(b, n):
                pe.wait_ge(s_R, b * KO * T + n + 1)
                for k in range(NBLK):
                    mm = t.matmul(bank[6 + k][:, 0:P], Joh[n % 2][:, k * P:(k + 1) * P], Roh[n % 2][:], start=False,
                                  stop=False)
                mm.then_inc(s_inv, 1)

            def batch(b):
                last = None if isinstance(b, int) else b - 1

                def turn(src, i, ready, done, free):
                    pe.wait_ge(ready, b * T + i + 1)
                    if some(b * T + i - 1 if i >= 2 else b * T):
                        pe.wait_ge(free, b * T + i - 1 if i >= 2 else b * T)
                    for c in range(ND):
                        mm = t.transpose(bank[i % 2][:, c * P:(c + 1) * P], src[:, c * P:(c + 1) * P], ident[:])
                    mm.then_inc(done, 1)

                def scores(i):
                    pe.wait_ge(s_xT, b * T + i + 1)
                    if i >= 2:
                        pe.wait_ge(s_pr, b * T + i - 1)
                    else:
                        if some(b * T):
                            pe.wait_ge(s_x1, b * T)
                    o = bank[2 + i % 2][:, 0:LC]
                    for c in range(ND):
                        t.matmul(o, xT[i % 2][:, c, :], KQ[c][:, ds(b * LC, LC)], start=c == 0, stop=False)
                    t.matmul(o, ones[0:1, :], cst[0:1, ds(b * LC, LC)], start=False, stop=True).then_inc(s_sc, 1)

                if some(b * T):
                    pe.wait_ge(s_xnT, b * T)
                for i in range(T):
                    turn(xhat[i], i, s_xhat, s_t1, s_xT)
                    if last is not None:
                        invert(last, 2 * i)
                        invert(last, 2 * i + 1)
                    if i >= 1:
                        scores(i - 1)
                scores(T - 1)
                norms(b, 0)

                def attend(i):
                    pe.wait_ge(s_prT, b * T + i + 1)
                    if i >= 2:
                        pe.wait_ge(s_x1, b * T + i - 1)
                    else:
                        pe.wait_ge(s_pr, (b + 1) * T)
                    t.matmul(bank[2 + i % 2][:, 0:D], prT[i % 2][0:LC, :], VO[0:LC, ds(b * D, D)], start=True,
                             stop=True).then_inc(s_o, 1)

                pe.wait_ge(s_xT, (b + 1) * T)
                for i in range(T):
                    pe.wait_ge(s_pr, b * T + i + 1)
                    if i >= 2:
                        pe.wait_ge(s_prT, b * T + i - 1)
                    t.transpose(bank[i % 2][0:LC, 0:P], pr[i], ident[:]).then_inc(s_p2, 1)
                    if i >= 1:
                        attend(i - 1)
                attend(T - 1)
                norms(b, 1)

                def logits(i):
                    pe.wait_ge(s_xnT, b * T + i + 1)
                    if i == 0:
                        if some(2 * b):
                            pe.wait_ge(s_ohp, 2 * b)
                    for c in range(ND):
                        mm = t.matmul(bank[4][:, i * E:(i + 1) * E], xT[i % 2][:, c, :], gw_s[:, c, :], start=c == 0,
                                      stop=c == ND - 1)
                    mm.then_inc(s_lg, 1)

                pe.wait_ge(s_prT, (b + 1) * T)
                for i in range(T):
                    turn(xext[:, i, :], i, s_xn, s_t2, s_xnT)
                    if i >= 1:
                        logits(i - 1)
                logits(T - 1)
                pe.wait_ge(s_m16, b + 1)
                pe.wait_ge(s_lgb, b + 1)
                if some(b):
                    pe.wait_ge(s_macc, b)
                pos = bank[4][:, 128:128 + T * E].rearrange("p (t e) -> p t e", t=T)
                t.matmul(pos, before16[:], msk16[:], start=True, stop=False)
                for j in range(1, T):
                    t.matmul(pos[:, j:T, :], ones16[:], msk16[:, 0:T - j, :], start=False, stop=False)
                t.matmul(pos, ones16[:], macc[:].rearrange("p (a e) -> p a e", a=1).to_broadcast([P, T, E]),
                         start=False, stop=True).then_inc(s_pos, 1)

            batch(0)
            with pe.Fori(1, B) as b:
                batch(b)

            for n in range(KO * T):
                invert(B - 1, n)
            for k in range(NBLK):
                mm = t.matmul(bank[6 + k][:, 0:P], zero16[:], zero16[:], start=False, stop=True)
            mm.then_inc(s_ltt, 1)
            pe.wait_ge(s_macc, B)
            t.matmul(bank[5][:, 0:E], ones16[:], macc[:], start=True, stop=True).then_inc(s_cnt, 1)
            pe.wait_ge(s_ltc, NBLK)
            pe.wait_ge(s_r1, 1)
            for k in range(NBLK):
                mm = t.matmul(bank[5][:, 128:128 + SP], LTT[:, k, :], Sel[:, k, :], start=k == 0, stop=k == NBLK - 1)
            mm.then_inc(s_idp, 1)

            pe.wait_ge(s_eid, 1)
            pe.wait_ge(s_lo, 2 * B)

            def turn_rows(s, u, i=None):
                pe.wait_ge(g_xg[u % U], (turn_of(s, u, i) + 1) * HT * 16)
                if some(s - 1):
                    pe.wait_ge(g_xl, s - 1)
                for c in range(ND):
                    for h in range(HT):
                        mm = t.transpose(bank[6 + u % 2][:, c * PS + h * P:c * PS + (h + 1) * P],
                                         xg[u % U][:, h, c * P:(c + 1) * P], ident[:])
                mm.then_inc(g_T, 1)

            def expert_of(s):
                return pe.value_load(eid[0:1, ds(s * HT, 1)], min_val=0, max_val=E - 1)

            def hidden(s, u, e):
                pb = u % 2
                pe.wait_ge(g_xl, s + 1)
                for j in range(NHB):
                    if some(NHB * (s - 1) + j + 1):
                        pe.wait_ge(g_hb, NHB * (s - 1) + j + 1)
                    for c2 in range(HC):
                        c = HC * j + c2
                        o = bank[j][:, c2 * PS:(c2 + 1) * PS]
                        for dc in range(ND):
                            at = ds(e * (ND * H) + (dc * H + c * P), P)
                            xs = slice(dc * PS, (dc + 1) * PS)
                            t.matmul(o, w1h[:, at], xh[pb][:, xs], start=dc == 0, stop=False)
                            t.matmul(o, w1h[:, at], xl[pb][:, xs], start=False, stop=False)
                            mm = t.matmul(o, w1l[:, at], xh[pb][:, xs], start=False, stop=dc == ND - 1)
                    mm.then_inc(g_mm1, 1)

            def output(s, u, e):
                pb = u % 2
                if some(s - 1):
                    pe.wait_ge(g_y1, s - 1)
                pe.wait_ge(g_hl, NHB * (s + 1))
                for h in range(HT):
                    o = bank[4 + pb][:, h * D:(h + 1) * D]
                    for c in range(NH):
                        at = ds(e * (NH * D) + c * D, D)
                        hs = slice(c * PS + h * P, c * PS + (h + 1) * P)
                        t.matmul(o, hh[pb][:, hs], w2h[:, at], start=c == 0, stop=False)
                        t.matmul(o, hh[pb][:, hs], w2l[:, at], start=False, stop=False)
                        mm = t.matmul(o, hl[pb][:, hs], w2h[:, at], start=False, stop=c == NH - 1)
                mm.then_inc(g_mm2, 1)

            turn_rows(0, 0)
            turn_rows(1, 1)
            hidden(0, 0, expert_of(0))

            def step(s, u, e, i=None):
                if not (isinstance(s, int) and s + 2 >= S):
                    turn_rows(s + 2, u + 2, i)
                after = None
                if not (isinstance(s, int) and s + 1 >= S):
                    after = expert_of(s + 1)
                    hidden(s + 1, u + 1, after)
                output(s, u, e)
                return after

            e = expert_of(0)
            for s in range(U):
                e = step(s, s, e)
            with pe.Fori(1, LOOPS) as i:
                e = expert_of(i * U)
                for u in range(U):
                    e = step(i * U + u, u, e, i)
            e = expert_of(LOOPS * U)
            for s in range(LOOPS * U, S):
                e = step(s, s % U, e)


_INS = ['x', 'ctx_768', 'g_xattn', 'g_ffn', 'L0_xattn_ln1_g', 'L0_xattn_ln1_b', 'L0_xattn_ln2_g', 'L0_xattn_ln2_b',
        'L0_xattn_Wq', 'L0_xattn_bq', 'L0_xattn_Wk', 'L0_xattn_bk', 'L0_xattn_Wv', 'L0_xattn_bv', 'L0_xattn_Wo',
        'L0_xattn_bo', 'L0_ffn_gate_w', 'L0_ffn_gate_b', 'L0_ffn_w1', 'L0_ffn_b1', 'L0_ffn_w2', 'L0_ffn_b2']
_OUTS = [((4, 1024, 256), 'float32')]


def kernel(**inputs):
    import numpy as _np
    import concourse.bacc as _bacc
    from concourse import mybir as _mybir
    from concourse.bass_utils import run_bass_kernel_spmd as _run

    nc = _bacc.Bacc("TRN2", target_bir_lowering=False, num_devices=1)
    arrays, args = {}, []
    for name in _INS:
        a = _np.ascontiguousarray(inputs[name])
        arrays[f"in_{name}_dram"] = a
        args.append(nc.dram_tensor(f"in_{name}_dram", a.shape, _mybir.dt.from_np(a.dtype), kind="ExternalInput").ap())
    for i, (shape, dtype) in enumerate(_OUTS):
        dt = _mybir.dt.from_np(_np.dtype(dtype))
        args.append(nc.dram_tensor(f"out_{i}_dram", shape, dt, kind="ExternalOutput").ap())
    gated_attention_and_routed_experts(nc, *args)
    r = _run(nc, [arrays], core_ids=[0])
    got = tuple(r.results[0][f"out_{i}_dram"] for i in range(len(_OUTS)))
    return got[0]
```
